# Optimizing a Trainium2 kernel written in Bass

```python
import numpy as np
import jax
import jax.numpy as jnp

def _softmax(x, axis=-1):
    return jax.nn.softmax(x, axis=axis)

def _gelu(x):
    return jax.nn.gelu(x, approximate=True)

def _silu(x):
    return jax.nn.silu(x)

def _sigmoid(x):
    return jax.nn.sigmoid(x)

def _layernorm(x, axis=-1, eps=1e-05):
    m = jnp.mean(x, axis=axis, keepdims=True)
    v = jnp.var(x, axis=axis, keepdims=True)
    return (x - m) / jnp.sqrt(v + eps)

def _scatter_add(tgt, idx, src, axis=0):
    return tgt.at[idx].add(src)

def _segment_sum(src, seg, n):
    return jax.ops.segment_sum(src, seg, n)
kernel_name = 'mk_adj_resnorm_d2_adj_r2_6525d8'

def setup_inputs(seed: int=0):
    np.random.seed(seed)
    _w = jnp.asarray

    def _rec_inputs():
        import jax
        import jax.numpy as jnp
        _gk = jax.random.key(seed)
        x = -0.000929 + 1 * jax.random.normal(jax.random.fold_in(_gk, 1), (4096, 128), jnp.float32)
        _w = (1.0 + jnp.arange(4096, dtype=jnp.float32)) ** (-0.5)
        _w = _w / _w.mean()
        _pij = jnp.clip(0.00195312 * _w[:, None] * _w[None, :], 0.0, 1.0)
        _a = jax.random.uniform(jax.random.fold_in(_gk, 2), (4096, 4096)) < _pij
        adj = _a.astype(jnp.int32)
        return (x, adj)
    x, adj = _rec_inputs()

    def _L0_gnn_setup():
        import jax, jax.numpy as jnp
        import numpy as np
        N = 4096
        IN = 128
        OUT = 128
        THR = 0.0001
        ALPHA = 0.2
        NEG = -1000000000.0
        key = jax.random.key(seed)
        k1, k2, k3, k4 = jax.random.split(key, 4)
        inp = jax.random.normal(k1, (N, IN), jnp.float32)
        W = jax.random.normal(k2, (IN, OUT), jnp.float32) * (1.414 * np.sqrt(2.0 / (IN + OUT)))
        a = jax.random.normal(k3, (2 * OUT, 1), jnp.float32) * (1.414 * np.sqrt(2.0 / (2 * OUT + 1)))
        adj = jax.random.randint(k4, (N, N), 0, 2, jnp.int32)
        return {'input': inp, 'W': W, 'a': a, 'adj': adj, 'M': N}
    _L0_gnn_all = _L0_gnn_setup()
    _L0_gnn_in = {k: v for k, v in _L0_gnn_all.items() if k in ('W', 'a')}
    del _L0_gnn_all

    def _L1_gnn_setup():
        import jax, jax.numpy as jnp
        import numpy as np
        NEG_BIG = -9000000000000000.0
        LEAKY_SLOPE = 0.2
        key = jax.random.key(seed)
        k1, k2, k3 = jax.random.split(key, 3)
        N, M, D = (4096, 4096, 128)
        qs = jax.random.normal(k1, (N, D), dtype=jnp.float32)
        ks = jax.random.normal(k2, (M, D), dtype=jnp.float32)
        HpGraph_e_k = jax.random.randint(k3, (N, M), 0, 2, dtype=jnp.int32)
        return {'qs': qs, 'ks': ks, 'HpGraph_e_k': HpGraph_e_k}
    _L1_gnn_all = _L1_gnn_setup()
    _L1_gnn_in = {k: v for k, v in _L1_gnn_all.items() if k in ('ks',)}
    del _L1_gnn_all
    return {'x': x, 'adj': adj, 'L0_gnn_W': _L0_gnn_in['W'], 'L0_gnn_a': _L0_gnn_in['a'], 'L1_gnn_ks': _L1_gnn_in['ks']}

def reference(x, adj, L0_gnn_W, L0_gnn_a, L1_gnn_ks):
    import jax
    import jax.numpy as jnp

    def _L0_gnn_ref(input, W, a, adj, M):
        import jax, jax.numpy as jnp
        import numpy as np
        N = 4096
        IN = 128
        OUT = 128
        THR = 0.0001
        ALPHA = 0.2
        NEG = -1000000000.0
        h = input @ W
        a_src = a[:OUT, 0]
        a_dst = a[OUT:, 0]
        e = jax.nn.leaky_relu((h[:M] @ a_src)[:, None] + (h @ a_dst)[None, :], negative_slope=ALPHA)
        valid = (adj[:M] > 0) & (h.sum(axis=1) != 0)[None, :]
        att = jax.nn.softmax(jnp.where(valid, e, NEG), axis=1)
        att = jnp.where(valid, att, 0.0)
        L = valid.sum(axis=1).astype(h.dtype)
        top = att.max(axis=1)
        attention = jnp.where(att >= THR, att, 0.0) * L[:, None]
        attention = jnp.where((top > THR)[:, None], attention, 0.0)
        h_prime = attention @ h
        return jax.nn.elu(h[:M] + h_prime)

    def _L1_gnn_ref(qs, ks, HpGraph_e_k):
        import jax, jax.numpy as jnp
        import numpy as np
        NEG_BIG = -9000000000000000.0
        LEAKY_SLOPE = 0.2
        scores = jnp.einsum('nd,md->nm', qs, ks)
        scores = jax.nn.leaky_relu(scores, negative_slope=LEAKY_SLOPE)
        scores = jnp.where(HpGraph_e_k > 0, scores, NEG_BIG)
        attn = jax.nn.softmax(scores, axis=1)
        return jnp.einsum('nm,md->nd', attn, ks)
    x = _layernorm(x + _L0_gnn_ref(x, L0_gnn_W, L0_gnn_a, adj, 4096), axis=-1)
    x = _layernorm(x + _L1_gnn_ref(x, L1_gnn_ks, adj), axis=-1)
    return x

_drawn_inputs = setup_inputs


def setup_inputs(seed=0):
    import zlib

    import numpy as np

    out = dict(_drawn_inputs(seed))
    spreads = {}
    factors = {}
    for name, (base, spread) in spreads.items():
        noise = np.random.default_rng([zlib.crc32(name.encode()), seed]).standard_normal(out[name].shape)
        drawn = base * np.exp(spread * noise) if base else spread * noise
        out[name] = jnp.asarray(drawn.astype(out[name].dtype))
    for name, factor in factors.items():
        out[name] = (out[name] * factor).astype(out[name].dtype)
    return out
```

```python
from contextlib import ExitStack

import concourse.bass as bass
from concourse import mybir

P = 128
CHUNK = 1024
BANK = 512
SLOTS = 3
SLOPE = 0.2
THR = 1e-4
EPS = 1e-5
NO_EDGE = 2.0 ** 100
ZERO_ROW = 2.0 ** 60
NO_ROW_MAX = 2.0 ** 50

ALU = mybir.AluOpType
ACT = mybir.ActivationFunctionType
AX = mybir.AxisListType
F32 = mybir.dt.float32
F16 = mybir.dt.float16
BF16 = mybir.dt.bfloat16
I32 = mybir.dt.int32


class Tile:

    def __init__(self, pair, off=0):
        self.pair, self.off = pair, off

    def __add__(self, k):
        return Tile(self.pair, self.off + k)

    @property
    def n(self):
        return self.pair * 2 + self.off

    @property
    def par(self):
        return self.off % 2

    @property
    def half(self):
        return self.pair + self.off // 2

    def count(self, per, k=0):
        return self.pair * (2 * per) + (self.off * per + k)


def graph_layers(nc, x, adj, W, a, ks, out):
    N, D = x.shape
    TILES = N // P
    BLOCKS = N // P
    CHUNKS = N // CHUNK
    PER = CHUNK // P
    assert D == P and TILES % 2 == 0 and CHUNKS == 4

    adj_rows = adj.rearrange("(t p) n -> t p n", p=P)
    x_rows = x.rearrange("(t p) d -> t p d", p=P)
    out_rows = out.rearrange("(t p) d -> t p d", p=P)

    with ExitStack() as ctx:
        def sb(name, shape, dt):
            return ctx.enter_context(nc.sbuf_tensor(name, shape, dt))

        def sem(name):
            return ctx.enter_context(nc.semaphore(name))

        def sem2(name):
            return [sem(name + "_even"), sem(name + "_odd")]

        adj_sb = [sb(f"adj_sb{i}", [P, N], I32) for i in range(2)]
        mask = [sb(f"mask{i}", [P, N], BF16) for i in range(2)]
        att0 = [sb(f"att0_{i}", [P, N], F32) for i in range(2)]
        att1 = sb("att1", [P, N], F32)
        att0T = sb("att0T", [P, N], F32)
        att1T = sb("att1T", [P, N], F32)
        d_all = sb("d_all", [P, N], F32)
        h_all = sb("h_all", [P, BLOCKS, D], F32)
        k_all = sb("k_all", [P, BLOCKS, D], F32)
        kT = sb("kT", [P, 2, N], F16)
        x_all = att0[1][:, :].rearrange("p (b d) -> p b d", d=D)
        xT = att1
        hT = att0T
        zero_row = att0[0]

        ident = sb("ident", [P, P], F32)
        ones = sb("ones", [P, P], F32)
        w_sb = sb("w_sb", [P, D], F32)
        a_sb = sb("a_sb", [P, 2], F32)
        a_dst_wide = sb("a_dst_wide", [P, P], F32)
        s_all = sb("s_all", [P, TILES], F32)
        neg_s_all = sb("neg_s_all", [P, TILES], F32)
        ident_b = sb("ident_b", [P, P], BF16)
        any_zero_f = sb("any_zero_f", [P, 1], F32)
        any_zero = sb("any_zero", [P, 1], I32)

        def pair(name, shape, dt=F32):
            return [sb(f"{name}{i}", shape, dt) for i in range(2)]

        top0 = pair("top0", [P, 1])
        neg0 = pair("neg0", [P, 1])
        lneg0 = pair("lneg0", [P, 1])
        bias0 = pair("bias0", [P, 1])
        absent = pair("absent", [P, 1])
        zeroed = pair("zeroed", [P, 1])
        z0 = pair("z0", [P, 1])
        cut0 = pair("cut0", [P, 1])
        z0_safe = pair("z0_safe", [P, 1])
        rz0 = pair("rz0", [P, 1])
        passes = pair("passes", [P, 1])
        edges = pair("edges", [P, 1])
        degree = pair("degree", [P, 1])
        coef0 = pair("coef0", [P, 1])
        top1 = pair("top1", [P, CHUNKS])
        bias1 = pair("bias1", [P, 1])
        z1 = pair("z1", [P, 1])
        rz1 = pair("rz1", [P, 1])
        x_sb = pair("x_sb", [P, D])
        y = pair("y", [P, D])
        y_neg = pair("y_neg", [P, D])
        y_exp = pair("y_exp", [P, D])
        y_pos = pair("y_pos", [P, D])
        y_posx = pair("y_posx", [P, D])
        res0 = pair("res0", [P, D])
        stat0 = pair("stat0", [P, 6])
        mv0 = pair("mv0", [P, 2])
        rstd0 = pair("rstd0", [P, 1])
        x1 = pair("x1", [P, D])
        qT = sb("qT", [P, 2, P], F16)
        res1 = pair("res1", [P, D])
        stat1 = pair("stat1", [P, 6])
        mv1 = pair("mv1", [P, 2])
        rstd1 = pair("rstd1", [P, 1])
        var0 = pair("var0", [P, 1])
        var1 = pair("var1", [P, 1])
        minus_half = sb("minus_half", [P, 1], F32)
        x2 = pair("x2", [P, D])

        work = ctx.enter_context(nc.psum_tensor("work", [P, SLOTS, CHUNK], F32))
        bank6 = ctx.enter_context(nc.psum_tensor("bank6", [P, BANK], F32))
        bank7 = ctx.enter_context(nc.psum_tensor("bank7", [P, BANK], F32))
        acc0 = bank6[:, 0:D]
        qT_ps = bank6[:, D:2 * D]
        s_ps = bank6[:, 2 * D:2 * D + TILES]
        acc1 = bank7[:, 0:D]

        adj_in, x_in, out_sent = sem2("adj_in"), sem2("x_in"), sem2("out_sent")
        small_in, xall_in, kall_in = sem("small_in"), sem("xall_in"), sem("kall_in")
        consts_zeroed, consts_ready, a_wide_ready = sem("consts_zeroed"), sem("consts_ready"), sem("a_wide_ready")
        setup_filled, setup_act, setup_dve = sem("setup_filled"), sem("setup_act"), sem("setup_dve")
        s_filled, s_ready = sem("s_filled"), sem("s_ready")
        zero_found, zero_max, zero_flag = sem("zero_found"), sem("zero_max"), sem("zero_flag")
        neg_s_ready, ident_b_ready = sem("neg_s_ready"), sem("ident_b_ready")
        mask_built, masked0, neg0_ready, lneg0_ready = sem("mask_built"), sem("masked0"), sem("neg0_ready"), sem("lneg0_ready")
        bias0_ready, bent0 = sem("bias0_ready"), sem("bent0")
        exp0 = sem("exp0")
        cut0_ready, z0_safe_ready, rz0_ready, cut_done = sem("cut0_ready"), sem("z0_safe_ready"), sem("rz0_ready"), sem("cut_done")
        passes_ready, edges_ready, degree_ready, coef0_ready = (
            sem("passes_ready"), sem("edges_ready"), sem("degree_ready"), sem("coef0_ready"))
        turned0, copied0, summed0 = sem("turned0"), sem("copied0"), sem("summed0")
        y_ready, y_neg_ready, y_exp_ready, y_pos_ready, y_posx_ready = (
            sem("y_ready"), sem("y_neg_ready"), sem("y_exp_ready"), sem("y_pos_ready"), sem("y_posx_ready"))
        res0_ready, stat0_ready, mv0_ready, rstd0_ready, x1_ready = (
            sem("res0_ready"), sem("stat0_ready"), sem("mv0_ready"), sem("rstd0_ready"), sem("x1_ready"))
        q_turned, q_high, q_low = sem("q_turned"), sem("q_high"), sem("q_low")
        scored, relu1, bent1, bias1_ready, exp1 = sem("scored"), sem("relu1"), sem("bent1"), sem("bias1_ready"), sem("exp1")
        turned1, copied1, summed1 = sem("turned1"), sem("copied1"), sem("summed1")
        rz1_ready, res1_ready, stat1_ready, mv1_ready, rstd1_ready, x2_ready = (
            sem("rz1_ready"), sem("res1_ready"), sem("stat1_ready"), sem("mv1_ready"),
            sem("rstd1_ready"), sem("x2_ready"))

        passed = sem("passed")
        var0_ready, var1_ready, minus_half_ready = sem("var0_ready"), sem("var1_ready"), sem("minus_half_ready")

        block = ctx.enter_context(nc.Block())

        def cols(c):
            return slice(c * CHUNK, (c + 1) * CHUNK)

        X_AT, K_AT, HT_AT, H_AT, D_AT = 0, CHUNKS, 2 * CHUNKS, 3 * CHUNKS, 4 * CHUNKS
        D_CHUNKS = N // BANK

        def wait_emptied(eng, n):
            if n < 0:
                return
            if n >= D_AT:
                eng.wait_ge(setup_dve, CHUNKS + n - D_AT + 1)
            elif K_AT <= n < HT_AT:
                eng.wait_ge(setup_dve, n - K_AT + 1)
            else:
                eng.wait_ge(setup_act, n + 1)

        def wait_apart(eng, semaphore, value):
            eng.wait_ge(semaphore, value)
            eng.sem_inc(passed, 1)

        def run_slots(eng, slot):
            slot(Tile(0, 0), ahead=True, layer0=True, layer1=False, last=False)
            slot(Tile(0, 1), ahead=True, layer0=True, layer1=True, last=False)
            for k in (2, 3):
                slot(Tile(0, k), ahead=True, layer0=True, layer1=True, last=True)
            with eng.Fori(2, TILES // 2 - 1) as i:
                slot(Tile(i, 0), ahead=True, layer0=True, layer1=True, last=True)
                slot(Tile(i, 1), ahead=True, layer0=True, layer1=True, last=True)
            end = Tile(TILES // 2 - 1, 0)
            slot(end, ahead=True, layer0=True, layer1=True, last=True)
            slot(end + 1, ahead=False, layer0=True, layer1=True, last=True)
            slot(end + 2, ahead=False, layer0=False, layer1=True, last=True)
            slot(end + 3, ahead=False, layer0=False, layer1=False, last=True)

        @block.sync
        def _(sp):
            sp.dma_start(x_all, x.rearrange("(b p) d -> p b d", p=P)).then_inc(xall_in, 16)
            sp.dma_start(w_sb[:, :], W).then_inc(small_in, 16)
            for i in range(2):
                sp.dma_start(a_sb[:, i:i + 1], a[i * D:(i + 1) * D, :]).then_inc(small_in, 16)
            sp.dma_start(k_all[:, :, :], ks.rearrange("(b p) d -> p b d", p=P)).then_inc(kall_in, 16)
            for t in range(2):
                sp.dma_start(adj_sb[t][:, :], adj_rows[t]).then_inc(adj_in[t], 16)
            sp.dma_start(x_sb[0][:, :], x_rows[0]).then_inc(x_in[0], 16)

            def load_adj(t):
                sp.wait_ge(bias0_ready, t.count(1, -1))
                sp.dma_start(adj_sb[t.par][:, :], adj_rows[t.n]).then_inc(adj_in[t.par], 16)

            def slot(t, ahead, layer0, layer1, last):
                if ahead:
                    if last or layer1:
                        sp.wait_ge(y_posx_ready, t.count(1))
                    sp.dma_start(x_sb[(t + 1).par][:, :], x_rows[(t + 1).n]).then_inc(x_in[(t + 1).par], 16)
                if last:
                    w = t + -2
                    sp.wait_ge(x2_ready, w.count(1, 1))
                    sp.dma_start(out_rows[w.n], x2[w.par][:, :]).then_inc(out_sent[w.par], 16)

            def slot_with_adj(t, **kinds):
                slot(t, **kinds)
                load_adj(t + 3)

            sp_first = [dict(ahead=True, layer0=True, layer1=False, last=False),
                        dict(ahead=True, layer0=True, layer1=True, last=False)]
            steady = dict(ahead=True, layer0=True, layer1=True, last=True)
            load_adj(Tile(0, 2))
            slot_with_adj(Tile(0, 0), **sp_first[0])
            slot_with_adj(Tile(0, 1), **sp_first[1])
            with sp.Fori(1, TILES // 2 - 2) as i:
                slot_with_adj(Tile(i, 0), **steady)
                slot_with_adj(Tile(i, 1), **steady)
            end = Tile(TILES // 2 - 2, 0)
            slot_with_adj(end, **steady)
            slot(end + 1, **steady)
            slot(end + 2, **steady)
            slot(end + 3, ahead=False, layer0=True, layer1=True, last=True)
            slot(end + 4, ahead=False, layer0=False, layer1=True, last=True)
            slot(end + 5, ahead=False, layer0=False, layer1=False, last=True)
            for p in range(2):
                sp.wait_ge(out_sent[p], 16 * (TILES // 2))

        @block.tensor
        def _(pe):
            def turn_x(c):
                wait_emptied(pe, X_AT + c - SLOTS)
                for b in range(PER):
                    mm = pe.transpose(work[:, (X_AT + c) % SLOTS, b * P:(b + 1) * P], x_all[:, c * PER + b, :],
                                      ident[:, :])
                mm.then_inc(setup_filled, 1)

            def turn_k(c):
                wait_emptied(pe, K_AT + c - SLOTS)
                for b in range(PER):
                    mm = pe.transpose(work[:, (K_AT + c) % SLOTS, b * P:(b + 1) * P], k_all[:, c * PER + b, :],
                                      ident[:, :])
                mm.then_inc(setup_filled, 1)

            def make_hT(c):
                pe.wait_ge(setup_act, X_AT + c + 1)
                wait_emptied(pe, HT_AT + c - SLOTS)
                for b in range(CHUNK // BANK):
                    lo = c * CHUNK + b * BANK
                    mm = pe.matmul(work[:, (HT_AT + c) % SLOTS, b * BANK:(b + 1) * BANK], w_sb[:, :],
                                   xT[:, lo:lo + BANK], start=True, stop=True)
                mm.then_inc(setup_filled, 1)

            def make_h(c):
                pe.wait_ge(setup_act, HT_AT + c + 1)
                wait_emptied(pe, H_AT + c - SLOTS)
                for b in range(PER):
                    lo = (c * PER + b) * P
                    mm = pe.transpose(work[:, (H_AT + c) % SLOTS, b * P:(b + 1) * P], hT[:, lo:lo + P], ident[:, :])
                mm.then_inc(setup_filled, 1)

            def make_d(c):
                wait_emptied(pe, D_AT + c - SLOTS)
                rhs = hT[:, c * BANK:(c + 1) * BANK]
                pe.matmul(work[:, (D_AT + c) % SLOTS, 0:BANK], ones[:, :], rhs, start=True, stop=True)
                pe.matmul(work[:, (D_AT + c) % SLOTS, BANK:CHUNK], a_dst_wide[:, :], rhs, start=True,
                          stop=True).then_inc(setup_filled, 1)

            pe.wait_ge(consts_ready, 2)
            pe.wait_ge(xall_in, 16)
            for c in range(CHUNKS):
                turn_x(c)
            pe.wait_ge(kall_in, 16)
            for c in range(CHUNKS):
                turn_k(c)
            pe.wait_ge(small_in, 48)
            for c in range(CHUNKS):
                make_hT(c)
            for c in range(CHUNKS):
                make_h(c)
            for b in range(BLOCKS):
                mm = pe.matmul(s_ps[:, b:b + 1], hT[:, b * P:(b + 1) * P], a_sb[:, 0:1], start=True, stop=True)
            mm.then_inc(s_filled, 1)
            pe.wait_ge(a_wide_ready, 1)
            for c in range(D_CHUNKS):
                make_d(c)
            pe.wait_ge(setup_dve, CHUNKS + D_CHUNKS)
            pe.wait_ge(ident_b_ready, 1)

            def score(u, c, first):
                pe.wait_ge(q_high, u.count(1, 1))
                pe.wait_ge(q_low, u.count(1, 1))
                if c < SLOTS:
                    if not first:
                        pe.wait_ge(copied1, u.count(4, c - 2))
                else:
                    pe.wait_ge(bent1, u.count(4, 1))
                pieces = [(work[:, c % SLOTS, b * BANK:(b + 1) * BANK],
                           slice(c * CHUNK + b * BANK, c * CHUNK + (b + 1) * BANK)) for b in range(CHUNK // BANK)]
                for o, part in pieces:
                    pe.matmul(o, ident_b[:, :], mask[u.par][:, part], start=True, stop=False)
                for o, part in pieces:
                    pe.matmul(o, qT[:, 0, :], kT[:, 0, part], start=False, stop=False)
                    pe.matmul(o, qT[:, 0, :], kT[:, 1, part], start=False, stop=False)
                for o, part in pieces:
                    mm = pe.matmul(o, qT[:, 1, :], kT[:, 0, part], start=False, stop=True)
                mm.then_inc(scored, 1)

            def turn0(t, c, layer1):
                pe.wait_ge(cut_done, t.count(2, 1 + c // 2))
                if c < 3:
                    if layer1:
                        pe.wait_ge(bent1, (t + -1).count(4, c + 2))
                else:
                    pe.wait_ge(copied0, t.count(4, 1))
                for b in range(PER):
                    lo = (c * PER + b) * P
                    mm = pe.transpose(work[:, (4 + c) % SLOTS, b * P:(b + 1) * P], att0[t.par][:, lo:lo + P],
                                      ident[:, :])
                mm.then_inc(turned0, 1)

            def sum0(t, c, layer1):
                pe.wait_ge(copied0, t.count(4, c + 1))
                if c == 0 and layer1:
                    pe.wait_ge(y_ready, t.count(1))
                for b in range(PER):
                    k = c * PER + b
                    mm = pe.matmul(acc0, att0T[:, k * P:(k + 1) * P], h_all[:, k, :], start=(k == 0),
                                   stop=(k == BLOCKS - 1))
                mm.then_inc(summed0, 1)

            def turn1(u, c, layer0):
                pe.wait_ge(exp1, u.count(1, 1))
                if c < 3:
                    if layer0:
                        pe.wait_ge(copied0, (u + 1).count(4, c + 2))
                else:
                    pe.wait_ge(copied1, u.count(4, 1))
                for b in range(PER):
                    lo = (c * PER + b) * P
                    mm = pe.transpose(work[:, (8 + c) % SLOTS, b * P:(b + 1) * P], att1[:, lo:lo + P], ident[:, :])
                mm.then_inc(turned1, 1)

            def sum1(u, c, first):
                pe.wait_ge(copied1, u.count(4, c + 1))
                if c == 0 and not first:
                    pe.wait_ge(res1_ready, u.count(1))
                for b in range(PER):
                    k = c * PER + b
                    mm = pe.matmul(acc1, att1T[:, k * P:(k + 1) * P], k_all[:, k, :], start=(k == 0),
                                   stop=(k == BLOCKS - 1))
                mm.then_inc(summed1, 1)

            def turn_q(t):
                pe.wait_ge(x1_ready, t.count(1, 1))
                pe.transpose(qT_ps, x1[t.par][:, :], ident[:, :]).then_inc(q_turned, 1)

            def slot(t, ahead, layer0, layer1, last):
                u = t + -1
                if layer1:
                    for c in range(CHUNKS):
                        score(u, c, not last)
                if layer0:
                    turn0(t, 0, layer1)
                    turn0(t, 1, layer1)
                    sum0(t, 0, layer1)
                    turn0(t, 2, layer1)
                    sum0(t, 1, layer1)
                    turn0(t, 3, layer1)
                    sum0(t, 2, layer1)
                if layer1:
                    turn1(u, 0, layer0)
                if layer0:
                    sum0(t, 3, layer1)
                if layer1:
                    turn1(u, 1, layer0)
                    sum1(u, 0, not last)
                    turn1(u, 2, layer0)
                    sum1(u, 1, not last)
                    turn1(u, 3, layer0)
                    sum1(u, 2, not last)
                if layer0:
                    turn_q(t)
                if layer1:
                    sum1(u, 3, not last)

            run_slots(pe, slot)

        @block.scalar
        def _(act):
            for c in range(CHUNKS):
                act.wait_ge(setup_filled, X_AT + c + 1)
                nc.scalar.copy(xT[:, cols(c)], work[:, (X_AT + c) % SLOTS, :]).then_inc(setup_act, 1)
            for c in range(CHUNKS):
                act.wait_ge(setup_filled, K_AT + c + 1)
                nc.scalar.copy(kT[:, 0, cols(c)], work[:, (K_AT + c) % SLOTS, :]).then_inc(setup_act, 1)
            for c in range(CHUNKS):
                act.wait_ge(setup_filled, HT_AT + c + 1)
                nc.scalar.copy(hT[:, cols(c)], work[:, (HT_AT + c) % SLOTS, :]).then_inc(setup_act, 1)
            for c in range(CHUNKS):
                act.wait_ge(setup_filled, H_AT + c + 1)
                nc.scalar.copy(h_all[:, c * PER:(c + 1) * PER, :], work[:, (H_AT + c) % SLOTS, :].rearrange(
                    "p (b d) -> p b d", d=D)).then_inc(setup_act, 1)

            def raise0(f):
                act.wait_ge(bent0, f.count(1, 1))
                act.wait_ge(bias0_ready, f.count(1, 1))
                b = att0[f.par]
                nc.scalar.activation(b[:, :], b[:, :], ACT.Exp, bias=bias0[f.par][:, :], scale=1.0 - SLOPE,
                                     accum_out=z0[f.par][:, :]).then_inc(exp0, 1)

            def copy0(t, c, layer1):
                act.wait_ge(turned0, t.count(4, c + 1))
                if layer1:
                    act.wait_ge(summed0, (t + -1).count(4, c + 1))
                nc.scalar.copy(att0T[:, cols(c)], work[:, (4 + c) % SLOTS, :]).then_inc(copied0, 1)

            def relu_part1(u, c, first):
                act.wait_ge(scored, u.count(4, c + 1))
                if c == 0 and not first:
                    act.wait_ge(turned1, u.count(4))
                nc.scalar.activation(att1[:, cols(c)], work[:, c % SLOTS, :], ACT.Relu,
                                     scale=1.0 / SLOPE - 1.0).then_inc(relu1, 1)

            def raise1(u):
                act.wait_ge(bent1, u.count(4, 4))
                act.wait_ge(bias1_ready, u.count(1, 1))
                nc.scalar.activation(att1[:, :], att1[:, :], ACT.Exp, bias=bias1[u.par][:, :],
                                     accum_out=z1[u.par][:, :]).then_inc(exp1, 1)

            def copy1(u, c, first):
                act.wait_ge(turned1, u.count(4, c + 1))
                if not first:
                    act.wait_ge(summed1, (u + -1).count(4, c + 1))
                nc.scalar.copy(att1T[:, cols(c)], work[:, (8 + c) % SLOTS, :]).then_inc(copied1, 1)

            def elu_exp(t):
                act.wait_ge(y_neg_ready, t.count(1, 1))
                nc.scalar.activation(y_exp[t.par][:, :], y_neg[t.par][:, :], ACT.Exp).then_inc(y_exp_ready, 1)

            def q_high_part(t):
                act.wait_ge(q_turned, t.count(1, 1))
                nc.scalar.copy(qT[:, 0, :], qT_ps).then_inc(q_high, 1)

            raise0(Tile(0))

            def slot(t, ahead, layer0, layer1, last):
                u, f = t + -1, t + 1
                if layer1:
                    for c in range(CHUNKS):
                        relu_part1(u, c, not last)
                if layer0:
                    copy0(t, 0, layer1)
                    copy0(t, 1, layer1)
                if layer0:
                    copy0(t, 2, layer1)
                    copy0(t, 3, layer1)
                if layer1:
                    raise1(u)
                    copy1(u, 0, not last)
                if layer0:
                    elu_exp(t)
                if layer1:
                    copy1(u, 1, not last)
                if ahead:
                    raise0(f)
                if layer1:
                    copy1(u, 2, not last)
                    copy1(u, 3, not last)
                if layer0:
                    q_high_part(t)

            run_slots(act, slot)

        @block.vector
        def _(dve):
            dve.wait_ge(small_in, 48)
            dve.wait_ge(consts_ready, 2)
            nc.vector.tensor_scalar(a_dst_wide[:, :], ones[:, :], a_sb[:, 1:2], None, ALU.mult).then_inc(a_wide_ready, 1)
            nc.vector.memset(zeroed[0][:, :], 0.0)
            nc.vector.memset(zeroed[1][:, :], 0.0)
            nc.vector.tensor_copy(ident_b[:, :], ident[:, :]).then_inc(ident_b_ready, 1)
            for c in range(CHUNKS):
                dve.wait_ge(setup_act, K_AT + c + 1)
                nc.vector.tensor_tensor(kT[:, 1, cols(c)], work[:, (K_AT + c) % SLOTS, :], kT[:, 0, cols(c)],
                                        ALU.subtract).then_inc(setup_dve, 1)
            dve.wait_ge(s_filled, 1)
            nc.vector.tensor_copy(s_all[:, :], s_ps).then_inc(s_ready, 1)
            nc.vector.tensor_scalar(neg_s_all[:, :], s_ps, -1.0, None, ALU.mult).then_inc(neg_s_ready, 1)
            for c in range(D_CHUNKS):
                dve.wait_ge(setup_filled, D_AT + c + 1)
                part = slice(c * BANK, (c + 1) * BANK)
                nc.vector.tensor_scalar(zero_row[:, part], work[:, (D_AT + c) % SLOTS, 0:BANK], 0.0, None,
                                        ALU.is_equal).then_inc(zero_found, 1)
                dve.wait_ge(zero_found, c + 1)
                nc.vector.scalar_tensor_tensor(d_all[:, part], zero_row[:, part], -ZERO_ROW,
                                               work[:, (D_AT + c) % SLOTS, BANK:CHUNK], ALU.mult,
                                               ALU.add).then_inc(setup_dve, 1)
            nc.vector.reduce_max(any_zero_f[:, :], zero_row[:, :], AX.X).then_inc(zero_max, 1)
            dve.wait_ge(zero_max, 1)
            nc.vector.tensor_copy(any_zero[:, :], any_zero_f[:, :]).then_inc(zero_flag, 1)
            dve.wait_ge(zero_flag, 1)
            dve.wait_ge(s_ready, 1)
            dve.wait_ge(neg_s_ready, 1)
            has_zero_rows = dve.value_load(any_zero[0:1, 0:1], min_val=0, max_val=1)
            dve.wait_ge(setup_dve, CHUNKS + D_CHUNKS)

            def ahead_of(f, first):
                p = f.par
                dve.wait_ge(adj_in[p], f.half * 16 + 16)
                nc.vector.tensor_scalar(mask[p][:, :], adj_sb[p][:, :], 0.0, -NO_EDGE, ALU.is_le,
                                        ALU.mult).then_inc(mask_built, 1)
                dve.wait_ge(mask_built, f.count(1, 1))
                if not first:
                    wait_apart(dve, turned0, f.count(4, -4))
                nc.vector.tensor_tensor_reduce(att0[p][:, :], mask[p][:, :], d_all[:, :], SLOPE / (1.0 - SLOPE),
                                               -3.0e38, ALU.add, ALU.max, top0[p][:, :]).then_inc(masked0, 1)
                dve.wait_ge(masked0, f.count(1, 1))
                nc.vector.scalar_tensor_tensor(att0[p][:, :], d_all[:, :], neg_s_all[:, bass.ds(f.n, 1)],
                                               att0[p][:, :], ALU.max, ALU.add,
                                               accum_out=absent[p][:, :]).then_inc(bent0, 1)
                nc.vector.tensor_scalar(neg0[p][:, :], top0[p][:, :], -(1.0 - SLOPE) / SLOPE,
                                        s_all[:, bass.ds(f.n, 1)], ALU.mult, ALU.subtract).then_inc(neg0_ready, 1)
                dve.wait_ge(neg0_ready, f.count(1, 1))
                nc.vector.scalar_tensor_tensor(lneg0[p][:, :], neg0[p][:, :], SLOPE, neg0[p][:, :], ALU.mult,
                                               ALU.min).then_inc(lneg0_ready, 1)
                wait_apart(dve, bent0, f.count(1, 1))
                with nc.vector.If(has_zero_rows):
                    nc.vector.tensor_scalar(adj_sb[p][:, :].bitcast(F32), att0[p][:, :],
                                            -ZERO_ROW * SLOPE / (1.0 - SLOPE), 0.0, ALU.is_equal, ALU.add,
                                            accum_out=zeroed[p][:, :])
                dve.wait_ge(lneg0_ready, f.count(1, 1))
                nc.vector.tensor_scalar(bias0[p][:, :], lneg0[p][:, :], NO_ROW_MAX, s_all[:, bass.ds(f.n, 1)],
                                        ALU.min, ALU.add).then_inc(bias0_ready, 1)

            def cut(t):
                p = t.par
                dve.wait_ge(exp0, t.count(1, 1))
                nc.vector.tensor_scalar(cut0[p][:, :], z0[p][:, :], THR, None, ALU.mult).then_inc(cut0_ready, 1)
                nc.vector.tensor_scalar(z0_safe[p][:, :], z0[p][:, :], 1e-30, None, ALU.max).then_inc(z0_safe_ready, 1)
                dve.wait_ge(cut0_ready, t.count(1, 1))
                for half in range(2):
                    part = slice(half * (N // 2), (half + 1) * (N // 2))
                    nc.vector.scalar_tensor_tensor(att0[p][:, part], att0[p][:, part], cut0[p][:, :],
                                                   att0[p][:, part], ALU.is_ge, ALU.mult).then_inc(cut_done, 1)
                dve.wait_ge(z0_safe_ready, t.count(1, 1))
                nc.vector.reciprocal(rz0[p][:, :], z0_safe[p][:, :]).then_inc(rz0_ready, 1)

            def bend1(u, c):
                wait_apart(dve, relu1, u.count(4, c + 1))
                nc.vector.tensor_tensor_reduce(att1[:, cols(c)], work[:, c % SLOTS, :], att1[:, cols(c)], SLOPE,
                                               -3.0e38, ALU.add, ALU.max,
                                               top1[u.par][:, c:c + 1]).then_inc(bent1, 1)

            def maximum1(u):
                dve.wait_ge(bent1, u.count(4, 4))
                nc.vector.tensor_reduce(bias1[u.par][:, :], top1[u.par][:, :], AX.X, ALU.max,
                                        negate=True).then_inc(bias1_ready, 1)

            def residual0(t):
                p = t.par
                dve.wait_ge(summed0, t.count(4, 4))
                dve.wait_ge(coef0_ready, t.count(1, 1))
                nc.vector.scalar_tensor_tensor(y[p][:, :], acc0, coef0[p][:, :], h_all[:, t.n, :], ALU.mult,
                                               ALU.add).then_inc(y_ready, 1)

            def norm0(t):
                p = t.par
                dve.wait_ge(res0_ready, t.count(1, 1))
                nc.vector.bn_stats(stat0[p][:, :], res0[p][:, :]).then_inc(stat0_ready, 1)
                wait_apart(dve, stat0_ready, t.count(1, 1))
                nc.vector.bn_aggr(mv0[p][:, :], stat0[p][:, :]).then_inc(mv0_ready, 1)

            def q_low_part(t):
                dve.wait_ge(q_high, t.count(1, 1))
                nc.vector.tensor_tensor(qT[:, 1, :], qT_ps, qT[:, 0, :], ALU.subtract).then_inc(q_low, 1)

            def finish1(w):
                p = w.par
                dve.wait_ge(exp1, w.count(1, 1))
                nc.vector.reciprocal(rz1[p][:, :], z1[p][:, :]).then_inc(rz1_ready, 1)
                dve.wait_ge(rz1_ready, w.count(1, 1))
                dve.wait_ge(summed1, w.count(4, 4))
                nc.vector.scalar_tensor_tensor(res1[p][:, :], acc1, rz1[p][:, :], x1[p][:, :], ALU.mult,
                                               ALU.add).then_inc(res1_ready, 1)
                dve.wait_ge(res1_ready, w.count(1, 1))
                nc.vector.bn_stats(stat1[p][:, :], res1[p][:, :]).then_inc(stat1_ready, 1)
                wait_apart(dve, stat1_ready, w.count(1, 1))
                nc.vector.bn_aggr(mv1[p][:, :], stat1[p][:, :]).then_inc(mv1_ready, 1)

            ahead_of(Tile(0), True)

            def slot(t, ahead, layer0, layer1, last):
                u, f, w = t + -1, t + 1, t + -2
                if layer0:
                    cut(t)
                if last:
                    finish1(w)
                if layer1:
                    for c in range(CHUNKS):
                        bend1(u, c)
                    maximum1(u)
                if ahead:
                    ahead_of(f, not layer1)
                if layer0:
                    residual0(t)
                    norm0(t)
                if layer0:
                    q_low_part(t)

            run_slots(dve, slot)

        @block.gpsimd
        def _(pool):
            nc.gpsimd.memset(minus_half[:, :], -0.5).then_inc(minus_half_ready, 1)
            nc.gpsimd.memset(ones[:, :], 1.0).then_inc(consts_ready, 1)
            nc.gpsimd.memset(ident[:, :], 0.0).then_inc(consts_zeroed, 1)
            pool.wait_ge(consts_zeroed, 1)
            nc.gpsimd.affine_select(out=ident[:, :], in_=ident[:, :], compare_op=ALU.not_equal, fill=1.0, base=0,
                                    pattern=[[-1, P]], channel_multiplier=1).then_inc(consts_ready, 1)

            def coefficient(t):
                p = t.par
                wait_apart(pool, bias0_ready, t.count(1, 1))
                nc.gpsimd.tensor_scalar(edges[p][:, :], absent[p][:, :], 1.0 / (NO_EDGE * SLOPE / (1.0 - SLOPE)),
                                        float(N), ALU.mult, ALU.add).then_inc(edges_ready, 1)
                wait_apart(pool, edges_ready, t.count(1, 1))
                nc.gpsimd.tensor_scalar(degree[p][:, :], edges[p][:, :], zeroed[p][:, :], None,
                                        ALU.subtract).then_inc(degree_ready, 1)
                wait_apart(pool, rz0_ready, t.count(1, 1))
                nc.gpsimd.tensor_scalar(passes[p][:, :], rz0[p][:, :], THR, None, ALU.is_gt).then_inc(passes_ready, 1)
                pool.wait_ge(degree_ready, t.count(1, 1))
                wait_apart(pool, passes_ready, t.count(1, 1))
                nc.gpsimd.tensor_scalar(coef0[p][:, :], degree[p][:, :], rz0[p][:, :], passes[p][:, :], ALU.mult,
                                        ALU.mult).then_inc(coef0_ready, 1)

            def elu(t):
                p = t.par
                wait_apart(pool, y_ready, t.count(1, 1))
                nc.gpsimd.tensor_scalar(y_neg[p][:, :], y[p][:, :], 0.0, None, ALU.min).then_inc(y_neg_ready, 1)
                nc.gpsimd.tensor_scalar(y_pos[p][:, :], y[p][:, :], 0.0, -1.0, ALU.max, ALU.add).then_inc(y_pos_ready, 1)
                pool.wait_ge(y_pos_ready, t.count(1, 1))
                pool.wait_ge(x_in[p], t.half * 16 + 16)
                nc.gpsimd.tensor_tensor(y_posx[p][:, :], y_pos[p][:, :], x_sb[p][:, :], ALU.add).then_inc(y_posx_ready, 1)
                pool.wait_ge(y_posx_ready, t.count(1, 1))
                pool.wait_ge(y_exp_ready, t.count(1, 1))
                nc.gpsimd.tensor_tensor(res0[p][:, :], y_posx[p][:, :], y_exp[p][:, :], ALU.add).then_inc(res0_ready, 1)

            def normalise0(t):
                p = t.par
                wait_apart(pool, mv0_ready, t.count(1, 1))
                nc.gpsimd.tensor_scalar(var0[p][:, :], mv0[p][:, 1:2], EPS, None, ALU.add).then_inc(var0_ready, 1)
                pool.wait_ge(var0_ready, t.count(1, 1))
                nc.gpsimd.tensor_tensor(rstd0[p][:, :], var0[p][:, :], minus_half[:, :],
                                        ALU.pow).then_inc(rstd0_ready, 1)
                wait_apart(pool, rstd0_ready, t.count(1, 1))
                nc.gpsimd.tensor_scalar(x1[p][:, :], res0[p][:, :], mv0[p][:, 0:1], rstd0[p][:, :], ALU.subtract,
                                        ALU.mult).then_inc(x1_ready, 1)

            def normalise1(w, first):
                p = w.par
                wait_apart(pool, mv1_ready, w.count(1, 1))
                nc.gpsimd.tensor_scalar(var1[p][:, :], mv1[p][:, 1:2], EPS, None, ALU.add).then_inc(var1_ready, 1)
                pool.wait_ge(var1_ready, w.count(1, 1))
                nc.gpsimd.tensor_tensor(rstd1[p][:, :], var1[p][:, :], minus_half[:, :],
                                        ALU.pow).then_inc(rstd1_ready, 1)
                pool.wait_ge(rstd1_ready, w.count(1, 1))
                if not first:
                    wait_apart(pool, out_sent[p], w.half * 16)
                nc.gpsimd.tensor_scalar(x2[p][:, :], res1[p][:, :], mv1[p][:, 0:1], rstd1[p][:, :], ALU.subtract,
                                        ALU.mult).then_inc(x2_ready, 1)

            pool.wait_ge(minus_half_ready, 1)

            def slot(t, ahead, layer0, layer1, last):
                if last:
                    normalise1(t + -2, isinstance(t.n, int) and t.n < 4)
                if layer0:
                    coefficient(t)
                    elu(t)
                    normalise0(t)

            run_slots(pool, slot)


def kernel(x, adj, L0_gnn_W, L0_gnn_a, L1_gnn_ks):
    import numpy as np
    import concourse.bacc as bacc
    from concourse.bass_utils import run_bass_kernel_spmd

    nc = bacc.Bacc("TRN2", target_bir_lowering=False, num_devices=1)
    given = {"x": x, "adj": adj, "W": L0_gnn_W, "a": L0_gnn_a, "ks": L1_gnn_ks}
    arrays = {name: np.ascontiguousarray(v) for name, v in given.items()}
    aps = [nc.dram_tensor(name, v.shape, mybir.dt.from_np(v.dtype), kind="ExternalInput").ap()
           for name, v in arrays.items()]
    out = nc.dram_tensor("out", arrays["x"].shape, F32, kind="ExternalOutput").ap()
    graph_layers(nc, *aps, out)
    r = run_bass_kernel_spmd(nc, [arrays], core_ids=[0])
    return r.results[0]["out"]
```
